# Optimizing a Trainium2 kernel written in Bass

```python
import numpy as np
import jax
import jax.numpy as jnp

def _softmax(x, axis=-1):
    return jax.nn.softmax(x, axis=axis)

def _gelu(x):
    return jax.nn.gelu(x, approximate=True)

def _silu(x):
    return jax.nn.silu(x)

def _sigmoid(x):
    return jax.nn.sigmoid(x)

def _layernorm(x, axis=-1, eps=1e-05):
    m = jnp.mean(x, axis=axis, keepdims=True)
    v = jnp.var(x, axis=axis, keepdims=True)
    return (x - m) / jnp.sqrt(v + eps)

def _scatter_add(tgt, idx, src, axis=0):
    return tgt.at[idx].add(src)

def _segment_sum(src, seg, n):
    return jax.ops.segment_sum(src, seg, n)
kernel_name = 'mk_perceiver_d1_seqx_r2_a12592'

def setup_inputs(seed: int=0):
    np.random.seed(seed)
    _w = jnp.asarray

    def _rec_inputs():
        import jax
        import jax.numpy as jnp
        _rk = jax.random.key(seed)
        x = 7.22e-05 + 1 * jax.random.normal(jax.random.fold_in(_rk, 1), (32, 32, 512), jnp.float32)
        _lenS = 32 - jax.random.randint(jax.random.fold_in(_rk, 7), (32,), 0, max(1, 32 // 4) + 1, jnp.int32)
        _lenS2 = 257 - jax.random.randint(jax.random.fold_in(_rk, 8), (32,), 0, max(1, 257 // 4) + 1, jnp.int32)
        _ctx_768P = jax.random.normal(jax.random.fold_in(_rk, 11), (32, 16, 384), jnp.float32)
        _ctx_768c = jax.random.dirichlet(jax.random.fold_in(_rk, 511), 0.3 * jnp.ones((16,), jnp.float32), (32, 257))
        _ctx_768t = jnp.einsum('bsk,bkd->bsd', _ctx_768c, _ctx_768P)
        _ctx_768t = _ctx_768t * jax.lax.rsqrt(jnp.mean(jnp.square(_ctx_768t)) + 1e-12) * 0.953939
        ctx_768 = 2.09791e-05 + 1.00001 * (_ctx_768t + 0.3 * jax.random.normal(jax.random.fold_in(_rk, 611), (32, 257, 384), jnp.float32))
        _validS = jnp.arange(32)[None, :] < _lenS[:, None]
        _validS2 = jnp.arange(257)[None, :] < _lenS2[:, None]
        _causal = jnp.tril(jnp.ones((32, 32), dtype=bool))
        mask_BxS_bk0 = jnp.logical_not(jnp.broadcast_to(_validS[:, :], (32, 32)))
        return (x, ctx_768, mask_BxS_bk0)
    x, ctx_768, mask_BxS_bk0 = _rec_inputs()

    def _L0_xattn_setup():
        import jax, jax.numpy as jnp
        import numpy as np
        NUM_HEADS = 16
        key = jax.random.key(seed)
        k1, k2, k3, k4, k5 = jax.random.split(key, 5)
        B, N, C = (4, 1024, 512)
        N2, Cy = (512, 384)
        x = jax.random.normal(k1, (B, N, C), dtype=jnp.float32)
        y = jax.random.normal(k2, (B, N2, Cy), dtype=jnp.float32)
        pad_mask = jax.random.randint(k3, (B, N), 0, 2).astype(jnp.bool_)
        Wq = jax.random.normal(k4, (C, C), dtype=jnp.float32) * C ** (-0.5)
        Wkv = jax.random.normal(k5, (2 * C, Cy), dtype=jnp.float32) * Cy ** (-0.5)
        return {'x': x, 'y': y, 'pad_mask': pad_mask, 'Wq': Wq, 'Wkv': Wkv}
    _L0_xattn_all = _L0_xattn_setup()
    _L0_xattn_in = {k: v for k, v in _L0_xattn_all.items() if k in ('Wq', 'Wkv')}
    del _L0_xattn_all

    def _L0_attn_setup():
        import jax, jax.numpy as jnp
        import numpy as np
        B, L, D, H, DK, DV = (2, 512, 512, 16, 64, 64)
        EPS = 1e-05

        def _silu(x):
            return x * jax.nn.sigmoid(x)
        key = jax.random.key(seed)
        ks = jax.random.split(key, 16)
        w = lambda k, shp: jax.random.normal(k, shp, dtype=jnp.float32) * 0.02
        return {'hidden_states': jax.random.normal(ks[0], (B, L, D), jnp.float32), 'Wq': w(ks[1], (D, H * DK)), 'bq': jnp.zeros((H * DK,), jnp.float32), 'Wk': w(ks[2], (D, H * DK)), 'bk': jnp.zeros((H * DK,), jnp.float32), 'Wv': w(ks[3], (D, H * DV)), 'bv': jnp.zeros((H * DV,), jnp.float32), 'Wb': w(ks[4], (D, H)), 'bb': jnp.zeros((H,), jnp.float32), 'Wfd': w(ks[5], (D, H)), 'bfd': jnp.zeros((H,), jnp.float32), 'fast_decay_bias': jnp.full((H,), -1.0, jnp.float32), 'Wsd': w(ks[6], (D, H)), 'bsd': jnp.zeros((H,), jnp.float32), 'slow_decay_bias': jnp.full((H,), 2.0, jnp.float32), 'Wfg': w(ks[7], (D, H)), 'bfg': jnp.zeros((H,), jnp.float32), 'Wsg': w(ks[8], (D, H)), 'bsg': jnp.zeros((H,), jnp.float32), 'Wg': w(ks[9], (D, H * DV)), 'bg': jnp.zeros((H * DV,), jnp.float32), 'onorm_w': jnp.ones((DV,), jnp.float32), 'Wo': w(ks[10], (H * DV, D)), 'bo': jnp.zeros((D,), jnp.float32), 'resonance_flux': jnp.float32(0.05)}
    _L0_attn_all = _L0_attn_setup()
    _L0_attn_in = {k: v for k, v in _L0_attn_all.items() if k in ('Wq', 'bq', 'Wk', 'bk', 'Wv', 'bv', 'Wb', 'bb', 'Wfd', 'bfd', 'fast_decay_bias', 'Wsd', 'bsd', 'slow_decay_bias', 'Wfg', 'bfg', 'Wsg', 'bsg', 'Wg', 'bg', 'onorm_w', 'Wo', 'bo', 'resonance_flux')}
    del _L0_attn_all

    def _L0_ffn_setup():
        import jax, jax.numpy as jnp
        import numpy as np
        NUM_EXPERTS = 8
        TOP_K = 2
        B, T, D, F = (4, 1024, 512, 1408)
        key = jax.random.key(seed)
        ks = jax.random.split(key, 5)
        return {'x': jax.random.normal(ks[0], (B, T, D), dtype=jnp.float32), 'router_w': jax.random.normal(ks[1], (D, NUM_EXPERTS), dtype=jnp.float32) * 0.02, 'gate_proj': jax.random.normal(ks[2], (NUM_EXPERTS, D, F), dtype=jnp.float32) * 0.02, 'up_proj': jax.random.normal(ks[3], (NUM_EXPERTS, D, F), dtype=jnp.float32) * 0.02, 'down_proj': jax.random.normal(ks[4], (NUM_EXPERTS, F, D), dtype=jnp.float32) * 0.02}
    _L0_ffn_all = _L0_ffn_setup()
    _L0_ffn_in = {k: v for k, v in _L0_ffn_all.items() if k in ('router_w', 'gate_proj', 'up_proj', 'down_proj')}
    del _L0_ffn_all
    return {'x': x, 'ctx_768': ctx_768, 'mask_BxS_bk0': mask_BxS_bk0, 'L0_xattn_Wq': _L0_xattn_in['Wq'], 'L0_xattn_Wkv': _L0_xattn_in['Wkv'], 'L0_attn_Wq': _L0_attn_in['Wq'], 'L0_attn_bq': _L0_attn_in['bq'], 'L0_attn_Wk': _L0_attn_in['Wk'], 'L0_attn_bk': _L0_attn_in['bk'], 'L0_attn_Wv': _L0_attn_in['Wv'], 'L0_attn_bv': _L0_attn_in['bv'], 'L0_attn_Wb': _L0_attn_in['Wb'], 'L0_attn_bb': _L0_attn_in['bb'], 'L0_attn_Wfd': _L0_attn_in['Wfd'], 'L0_attn_bfd': _L0_attn_in['bfd'], 'L0_attn_fast_decay_bias': _L0_attn_in['fast_decay_bias'], 'L0_attn_Wsd': _L0_attn_in['Wsd'], 'L0_attn_bsd': _L0_attn_in['bsd'], 'L0_attn_slow_decay_bias': _L0_attn_in['slow_decay_bias'], 'L0_attn_Wfg': _L0_attn_in['Wfg'], 'L0_attn_bfg': _L0_attn_in['bfg'], 'L0_attn_Wsg': _L0_attn_in['Wsg'], 'L0_attn_bsg': _L0_attn_in['bsg'], 'L0_attn_Wg': _L0_attn_in['Wg'], 'L0_attn_bg': _L0_attn_in['bg'], 'L0_attn_onorm_w': _L0_attn_in['onorm_w'], 'L0_attn_Wo': _L0_attn_in['Wo'], 'L0_attn_bo': _L0_attn_in['bo'], 'L0_attn_resonance_flux': _L0_attn_in['resonance_flux'], 'L0_ffn_router_w': _L0_ffn_in['router_w'], 'L0_ffn_gate_proj': _L0_ffn_in['gate_proj'], 'L0_ffn_up_proj': _L0_ffn_in['up_proj'], 'L0_ffn_down_proj': _L0_ffn_in['down_proj']}

def reference(x, ctx_768, mask_BxS_bk0, L0_xattn_Wq, L0_xattn_Wkv, L0_attn_Wq, L0_attn_bq, L0_attn_Wk, L0_attn_bk, L0_attn_Wv, L0_attn_bv, L0_attn_Wb, L0_attn_bb, L0_attn_Wfd, L0_attn_bfd, L0_attn_fast_decay_bias, L0_attn_Wsd, L0_attn_bsd, L0_attn_slow_decay_bias, L0_attn_Wfg, L0_attn_bfg, L0_attn_Wsg, L0_attn_bsg, L0_attn_Wg, L0_attn_bg, L0_attn_onorm_w, L0_attn_Wo, L0_attn_bo, L0_attn_resonance_flux, L0_ffn_router_w, L0_ffn_gate_proj, L0_ffn_up_proj, L0_ffn_down_proj):
    import jax
    import jax.numpy as jnp

    def _L0_xattn_ref(x, y, pad_mask, Wq, Wkv):
        import jax, jax.numpy as jnp
        import numpy as np
        NUM_HEADS = 16
        B, N, C = x.shape
        N2 = y.shape[1]
        H = NUM_HEADS
        d = C // H
        scale = d ** (-0.5)
        q = (x @ Wq.T).reshape(B, N, H, d).transpose(0, 2, 1, 3)
        kv = (y @ Wkv.T).reshape(B, N2, 2, H, d).transpose(2, 0, 3, 1, 4)
        k, v = (kv[0], kv[1])
        attn = jnp.einsum('bhnd,bhmd->bhnm', q * scale, k)
        attn = jnp.where(pad_mask[:, None, :, None], attn, jnp.float32(-1000000000.0))
        attn = jax.nn.softmax(attn, axis=-1)
        out = jnp.einsum('bhnm,bhmd->bhnd', attn, v)
        return out.transpose(0, 2, 1, 3).reshape(B, N, C)

    def _L0_attn_ref(hidden_states, Wq, bq, Wk, bk, Wv, bv, Wb, bb, Wfd, bfd, fast_decay_bias, Wsd, bsd, slow_decay_bias, Wfg, bfg, Wsg, bsg, Wg, bg, onorm_w, Wo, bo, resonance_flux):
        import jax, jax.numpy as jnp
        import numpy as np
        B, L, D, H, DK, DV = (2, 512, 512, 16, 64, 64)
        EPS = 1e-05

        def _silu(x):
            return x * jax.nn.sigmoid(x)
        Bn, Ln, Dn = hidden_states.shape
        hs = hidden_states
        q = _silu(hs @ Wq + bq).reshape(Bn, Ln, H, DK).transpose(0, 2, 1, 3)
        k = _silu(hs @ Wk + bk).reshape(Bn, Ln, H, DK).transpose(0, 2, 1, 3)
        v = _silu(hs @ Wv + bv).reshape(Bn, Ln, H, DV).transpose(0, 2, 1, 3)
        beta = jax.nn.sigmoid(hs @ Wb + bb).transpose(0, 2, 1)
        fd = jax.nn.sigmoid(hs @ Wfd + bfd + fast_decay_bias).transpose(0, 2, 1)
        sd = jax.nn.sigmoid(hs @ Wsd + bsd + slow_decay_bias).transpose(0, 2, 1)
        fg = jax.nn.sigmoid(hs @ Wfg + bfg).transpose(0, 2, 1)
        sg = jax.nn.sigmoid(hs @ Wsg + bsg).transpose(0, 2, 1)
        q = q * jax.lax.rsqrt(jnp.sum(q * q, axis=-1, keepdims=True) + 1e-06)
        k = k * jax.lax.rsqrt(jnp.sum(k * k, axis=-1, keepdims=True) + 1e-06)
        xs = (q.transpose(2, 0, 1, 3), k.transpose(2, 0, 1, 3), v.transpose(2, 0, 1, 3), beta.transpose(2, 0, 1), fd.transpose(2, 0, 1), sd.transpose(2, 0, 1), fg.transpose(2, 0, 1), sg.transpose(2, 0, 1))
        S0 = jnp.zeros((Bn, H, DK, DV), hs.dtype)
        rf = resonance_flux

        def _cap(S):
            n = jnp.sqrt(jnp.sum(S * S, axis=(-2, -1), keepdims=True))
            return S / jnp.maximum(1.0, n / float(DK))

        def step(carry, x):
            S_f, S_s = carry
            qt, kt, vt, bt, fdt, sdt, fgt, sgt = x
            S_f = fdt[..., None, None] * S_f
            S_s = sdt[..., None, None] * S_s
            err_f = vt - jnp.einsum('bhk,bhkv->bhv', kt, S_f)
            err_s = vt - jnp.einsum('bhk,bhkv->bhv', kt, S_s)
            bkt = bt[..., None, None] * kt[..., :, None]
            S_f = S_f + bkt * err_f[..., None, :]
            S_s = S_s + bkt * err_s[..., None, :]
            S_fc = _cap(S_f + rf * S_s)
            S_sc = _cap(S_s + rf * S_f)
            ot = fgt[..., None] * jnp.einsum('bhk,bhkv->bhv', qt, S_fc) + sgt[..., None] * jnp.einsum('bhk,bhkv->bhv', qt, S_sc)
            return ((S_fc, S_sc), ot)
        _, o = jax.lax.scan(step, (S0, S0), xs)
        o = o.transpose(1, 0, 2, 3)
        g = (hs @ Wg + bg).reshape(Bn, Ln, H, DV)
        o = o * jax.lax.rsqrt(jnp.mean(o * o, axis=-1, keepdims=True) + EPS)
        o = o * onorm_w * _silu(g)
        o = o.reshape(Bn, Ln, H * DV) @ Wo + bo
        return o

    def _L0_ffn_ref(x, router_w, gate_proj, up_proj, down_proj):
        import jax, jax.numpy as jnp
        import numpy as np
        NUM_EXPERTS = 8
        TOP_K = 2
        B, T, D, F = (4, 1024, 512, 1408)
        scores = jnp.einsum('btd,de->bte', x, router_w).astype(jnp.float32)
        probs = jax.nn.softmax(scores, axis=-1)
        routing_weights, routing_idx = jax.lax.top_k(probs, TOP_K)
        routing_weights = (routing_weights / jnp.sum(routing_weights, axis=-1, keepdims=True)).astype(x.dtype)
        one_hot = jax.nn.one_hot(routing_idx, NUM_EXPERTS, dtype=x.dtype)
        expert_w = jnp.einsum('btke,btk->bte', one_hot, routing_weights)
        dispatched = jnp.einsum('btd,btke->bted', x, one_hot)
        gate = jnp.einsum('bted,edf->btef', dispatched, gate_proj)
        up = jnp.einsum('bted,edf->btef', dispatched, up_proj)
        acts = jax.nn.silu(gate) * up
        expert_out = jnp.einsum('btef,efd->bted', acts, down_proj)
        return jnp.einsum('bted,bte->btd', expert_out, expert_w)
    x = x + _L0_xattn_ref(_layernorm(x, axis=-1), ctx_768, mask_BxS_bk0, L0_xattn_Wq, L0_xattn_Wkv)
    x = x + _L0_attn_ref(_layernorm(x, axis=-1), L0_attn_Wq, L0_attn_bq, L0_attn_Wk, L0_attn_bk, L0_attn_Wv, L0_attn_bv, L0_attn_Wb, L0_attn_bb, L0_attn_Wfd, L0_attn_bfd, L0_attn_fast_decay_bias, L0_attn_Wsd, L0_attn_bsd, L0_attn_slow_decay_bias, L0_attn_Wfg, L0_attn_bfg, L0_attn_Wsg, L0_attn_bsg, L0_attn_Wg, L0_attn_bg, L0_attn_onorm_w, L0_attn_Wo, L0_attn_bo, L0_attn_resonance_flux)
    x = x + _L0_ffn_ref(_layernorm(x, axis=-1), L0_ffn_router_w, L0_ffn_gate_proj, L0_ffn_up_proj, L0_ffn_down_proj)
    return x

_drawn_inputs = setup_inputs


def setup_inputs(seed=0):
    import zlib

    import numpy as np

    out = dict(_drawn_inputs(seed))
    spreads = {'L0_attn_bq': (0.0, 0.1),
     'L0_attn_bk': (0.0, 0.1),
     'L0_attn_bv': (0.0, 0.1),
     'L0_attn_bb': (0.0, 2.0),
     'L0_attn_bfd': (0.0, 2.0),
     'L0_attn_fast_decay_bias': (-1.0, 0.6),
     'L0_attn_bsd': (0.0, 2.0),
     'L0_attn_slow_decay_bias': (2.0, 0.6),
     'L0_attn_bfg': (0.0, 2.0),
     'L0_attn_bsg': (0.0, 2.0),
     'L0_attn_bg': (0.0, 0.1),
     'L0_attn_onorm_w': (1.0, 0.6),
     'L0_attn_bo': (0.0, 0.1)}
    factors = {'L0_attn_Wb': 2.87,
     'L0_attn_Wfd': 8.0,
     'L0_attn_Wsd': 4.966,
     'L0_attn_Wfg': 8.0,
     'L0_attn_Wsg': 8.0}
    for name, (base, spread) in spreads.items():
        noise = np.random.default_rng([zlib.crc32(name.encode()), seed]).standard_normal(out[name].shape)
        drawn = base * np.exp(spread * noise) if base else spread * noise
        out[name] = jnp.asarray(drawn.astype(out[name].dtype))
    for name, factor in factors.items():
        out[name] = (out[name] * factor).astype(out[name].dtype)
    return out
```

```python
from contextlib import ExitStack

import concourse.bass as bass
from concourse import mybir

F32 = mybir.dt.float32
F32R = mybir.dt.float32r
U8 = mybir.dt.uint8
ALU = mybir.AluOpType
ACT = mybir.ActivationFunctionType
AX = mybir.AxisListType

P = 128
B, N, C = 32, 32, 512
TOK = B * N
NT = TOK // P
BT = P // N
KC = C // P
M, CY = 257, 384
KY = CY // P
HX, DX = 16, 32
HG = P // DX
H, DK = 16, 64
HC = H * DK // P
HALF = TOK // 2
TH = HALF // P
BH = B // 2
SG = BH * H // P
BS = P // H
E, F = 8, 1408
FC = F // P
NG = 5
EPS = 1e-5


class Chain:

    def __init__(self, eng, sem):
        self.eng, self.sem, self.n, self.base = eng, sem, 0, 0

    def link(self, ins):
        self.n += 1
        ins.then_inc(self.sem, 1)
        self.eng.wait_ge(self.sem, self.base + self.n)


def layer_norm(nc, tag, x_nat, xnT, ident, psum, row_scale=None, residual_T=None, before=None, after=None):
    with ExitStack() as ctx:
        sb = lambda name, shape: ctx.enter_context(nc.sbuf_tensor(tag + name, shape, F32))
        sem = lambda name: ctx.enter_context(nc.semaphore(tag + name))
        stats, mv = sb("stats", [P, NT, 6]), sb("mv", [P, NT, 2])
        var, std, rs = sb("var", [P, NT]), sb("std", [P, NT]), sb("rs", [P, NT])
        xn = sb("xn", [P, NT, C])
        own, added, res_ready, var_ready, std_ready = sem("own"), sem("added"), sem("res"), sem("varr"), sem("stdr")
        xn_ready, tr_done, copied = sem("xnr"), sem("tr"), sem("cp")
        b = before or {}
        with nc.Block() as block:
            @block.sync
            def _(sp):
                if "sync" in b:
                    b["sync"](sp)

            @block.gpsimd
            def _(pool):
                if "gpsimd" in b:
                    b["gpsimd"](pool)

            @block.vector
            def _(dve):
                ch = Chain(dve, own)
                if "vector" in b:
                    b["vector"](dve, ch)
                for t in range(NT):
                    if residual_T is not None:
                        dve.wait_ge(res_ready, t + 1)
                        nc.vector.tensor_tensor(x_nat[:, t, :], x_nat[:, t, :], psum[2 + t % 2], ALU.add).then_inc(added, 1)
                        dve.wait_ge(added, t + 1)
                    ins = nc.vector.bn_stats(stats[:, t, :], x_nat[:, t, :])
                ch.link(ins)
                for t in range(NT):
                    ins = nc.vector.bn_aggr(mv[:, t, :], stats[:, t, :])
                ch.link(ins)
                nc.vector.tensor_scalar(var[:, :], mv[:, :, 1], EPS, None, ALU.add).then_inc(var_ready, 1)
                dve.wait_ge(std_ready, 1)
                ch.link(nc.vector.reciprocal(rs[:, :], std[:, :]))
                if row_scale is not None:
                    ch.link(nc.vector.tensor_tensor(rs[:, :], rs[:, :], row_scale, ALU.mult))
                for t in range(NT):
                    nc.vector.tensor_scalar(xn[:, t, :], x_nat[:, t, :], mv[:, t, 0:1], rs[:, t:t + 1],
                                            ALU.subtract, ALU.mult).then_inc(xn_ready, 1)

            @block.scalar
            def _(act):
                act.wait_ge(var_ready, 1)
                nc.scalar.activation(std[:, :], var[:, :], ACT.Sqrt).then_inc(std_ready, 1)
                for t in range(NT):
                    act.wait_ge(tr_done, t + 1)
                    nc.scalar.copy(xnT[:, :, t * P:(t + 1) * P],
                                   psum[t % 2].rearrange("p (k n) -> p k n", k=KC)).then_inc(copied, 1)

            @block.tensor
            def _(pe):
                if "tensor" in b:
                    b["tensor"](pe)
                if residual_T is not None:
                    for t in range(NT):
                        if t >= 2:
                            pe.wait_ge(added, t - 1)
                        for k in range(KC):
                            mm = pe.transpose(psum[2 + t % 2][:, k * P:(k + 1) * P],
                                              residual_T[:, k, t * P:(t + 1) * P], ident[:, :])
                        mm.then_inc(res_ready, 1)
                for t in range(NT):
                    pe.wait_ge(xn_ready, t + 1)
                    if t >= 2:
                        pe.wait_ge(copied, t - 1)
                    for k in range(KC):
                        mm = pe.transpose(psum[t % 2][:, k * P:(k + 1) * P], xn[:, t, k * P:(k + 1) * P], ident[:, :])
                    mm.then_inc(tr_done, 1)
                if after is not None:
                    pe.wait_ge(copied, NT)
                    after(pe)


def cross_attention(nc, d, ps, ident, x_nat, xnT, mask_scale):
    with ExitStack() as ctx:
        sb = lambda name, shape: ctx.enter_context(nc.sbuf_tensor(name, shape, F32))
        sem = lambda name: ctx.enter_context(nc.semaphore(name))
        wq = sb("xa_wq", [P, KC, C])
        wkv = sb("xa_wkv", [P, KY, 2 * C])
        ctx_last = sb("ctx_last", [P, KY, B])
        v_last = sb("v_last", [B, C])
        block_mask = sb("block_mask", [P, HG, N])
        qT = sb("qT", [P, KC, TOK])
        oT = sb("oT", [P, KC, TOK])

        mask_u8 = ctx.enter_context(nc.sbuf_tensor("mask_u8", [P, NT], U8))
        x_in, w_in, consts, vl_done, vl_copied, vl_out = (sem("x_in"), sem("xw_in"), sem("consts"), sem("vl_done"),
                                                          sem("vl_copied"), sem("vl_out"))

        def load(sp):
            sp.dma_start(x_nat[:, :, :], d["x"].rearrange("(t p) c -> p t c", p=P)).then_inc(x_in, 16)
            sp.dma_start(mask_u8[:, :], d["mask"]).then_inc(x_in, 16)
            sp.dma_start(wkv[:, :, :], d["wkvT"].rearrange("(k p) n -> p k n", p=P)).then_inc(w_in, 16)
            sp.dma_start(ctx_last[:, :, :], d["ctx_last"].rearrange("(k p) n -> p k n", p=P)).then_inc(w_in, 16)
            sp.dma_start(wq[:, :, :], d["wqT"].rearrange("(k p) n -> p k n", p=P)).then_inc(w_in, 16)
            sp.wait_ge(w_in, 48)
            sp.wait_ge(vl_copied, 1)
            sp.dma_start(d["v_last"], v_last[:, :]).then_inc(vl_out, 16)

        def constants(pool):
            ones = nc.gpsimd.memset(ident[:, :], 0.0)
            ones.then_inc(consts, 1)
            pool.wait_ge(consts, 1)
            nc.gpsimd.affine_select(out=ident[:, :], in_=ident[:, :], compare_op=ALU.not_equal, fill=1.0, base=0,
                                    pattern=[[-1, P]], channel_multiplier=1).then_inc(consts, 1)
            nc.gpsimd.memset(block_mask[:, :, :], 0.0).then_inc(consts, 1)
            pool.wait_ge(consts, 3)
            for h in range(HG):
                nc.gpsimd.memset(block_mask[h * DX:(h + 1) * DX, h, :], 1.0).then_inc(consts, 1)

        def mask_rows(dve, ch):
            dve.wait_ge(x_in, 32)
            ch.link(nc.vector.tensor_copy(mask_scale[:, :], mask_u8[:, :]))
            ch.link(nc.vector.tensor_scalar(mask_scale[:, :], mask_scale[:, :], DX ** -0.5, None, ALU.mult))
            dve.wait_ge(vl_done, 1)
            nc.vector.tensor_copy(v_last[:, :], ps[7][0:B, :]).then_inc(vl_copied, 1)

        def last_values(pe):
            pe.wait_ge(w_in, 48)
            pe.wait_ge(consts, 2)
            for k in range(KY):
                mm = pe.matmul(ps[7][0:B, :], ctx_last[:, k, :], wkv[:, k, C:2 * C], start=(k == 0), stop=(k == KY - 1))
            mm.then_inc(vl_done, 1)

        layer_norm(nc, "n1_", x_nat, xnT, ident, ps, row_scale=mask_scale[:, :],
                   before={"sync": load, "gpsimd": constants, "vector": mask_rows, "tensor": last_values})

        q_done, q_copied = sem("q_done"), sem("q_copied")
        with nc.Block() as block:
            @block.tensor
            def _(pe):
                for i in range(2 * KC):
                    c, hf = i % KC, i // KC
                    if i >= 4:
                        pe.wait_ge(q_copied, i - 3)
                    for k in range(KC):
                        mm = pe.matmul(ps[i % 4], wq[:, k, c * P:(c + 1) * P], xnT[:, k, hf * HALF:(hf + 1) * HALF],
                                       start=(k == 0), stop=(k == KC - 1))
                    mm.then_inc(q_done, 1)

            @block.vector
            def _(dve):
                for i in range(2 * KC):
                    c, hf = i % KC, i // KC
                    dve.wait_ge(q_done, i + 1)
                    nc.vector.tensor_copy(qT[:, c, hf * HALF:(hf + 1) * HALF], ps[i % 4]).then_inc(q_copied, 1)

        attend(nc, d, ps, ident, wkv, block_mask, qT, oT, vl_out)
        layer_norm(nc, "n2_", x_nat, xnT, ident, ps, residual_T=oT)


def attend(nc, d, ps, ident, wkv, block_mask, qT, oT, vl_out):
    with ExitStack() as ctx:
        sb = lambda name, shape: ctx.enter_context(nc.sbuf_tensor(name, shape, F32))
        sem = lambda name: ctx.enter_context(nc.semaphore(name))
        ctxT = [sb(f"ctxT{s}", [P, KY, M]) for s in range(2)]
        kT = [sb(f"xkT{s}", [P, KC, M]) for s in range(2)]
        val = [sb(f"xv{s}", [P, 2, C]) for s in range(2)]
        v_tail = [sb(f"v_tail{s}", [1, C]) for s in range(2)]
        q_blocks = [sb(f"q_blocks{s}", [P, KC, HG, N]) for s in range(2)]
        prob = [sb(f"prob{s}", [P, KC, M]) for s in range(2)]
        probT = [sb(f"probT{s}", [P, 2, C]) for s in range(2)]
        probT_tail = [sb(f"probT_tail{s}", [1, C]) for s in range(2)]
        neg_max = [sb(f"neg_max{s}", [P, KC]) for s in range(2)]
        total = [sb(f"total{s}", [P, KC]) for s in range(2)]
        o_masked = sb("o_masked", [P, KC, HG, N])
        ctx_in = [sem(f"ctx_in{s}") for s in range(2)]
        k_done, k_copied, v_done, v_copied = sem("k_done"), sem("k_copied"), sem("v_done"), sem("v_copied")
        s_done, max_done, exp_done, norm_done = sem("s_done"), sem("max_done"), sem("exp_done"), sem("norm_done")
        t_done, t_copied, o_done, o_taken, qb_done = sem("t_done"), sem("t_copied"), sem("o_done"), sem("o_taken"), sem("qb_done")
        recip_done, masked_done = sem("recip_done"), sem("masked_done")

        def batches(eng, step):
            step(0, 0, 0)
            with eng.Fori(0, B // 2 - 1) as i:
                step(i * 2 + 1, 1, i)
                step(i * 2 + 2, 0, i + 1)
            step(B - 1, 1, B // 2 - 1)

        first = lambda b: isinstance(b, int) and b == 0

        with nc.Block() as block:
            @block.sync
            def _(sp):
                def step(b, s):
                    sp.dma_start(ctxT[s][:, :, :], d["ctxT"][bass.ds(b, 1), :, :].rearrange("a (k p) m -> p (a k) m", p=P)
                                 ).then_inc(ctx_in[s], 16)
                    sp.dma_start(v_tail[s][:, :], d["v_last"][bass.ds(b, 1), :]).then_inc(ctx_in[s], 16)

                sp.wait_ge(vl_out, 16)
                for b in range(B):
                    if b >= 2:
                        sp.wait_ge(k_done, (b - 1) * KC)
                        sp.wait_ge(v_done, (b - 1) * 2)
                        sp.wait_ge(o_done, b - 1)
                    step(b, b % 2)

            @block.tensor
            def _(pe):
                def keys_values(b, s, r):
                    pe.wait_ge(ctx_in[s], (r + 1) * 32)
                    for c in range(KC):
                        if not first(b):
                            pe.wait_ge(exp_done, (b - 1) * KC + c + 1)
                        for k in range(KY):
                            mm = pe.matmul(ps[c][:, 0:M], wkv[:, k, c * P:(c + 1) * P], ctxT[s][:, k, :],
                                           start=(k == 0), stop=(k == KY - 1))
                        mm.then_inc(k_done, 1)
                    if not (isinstance(b, int) and b < 2):
                        pe.wait_ge(t_copied, (b - 1) * 3)
                    for m in range(2):
                        for k in range(KY):
                            mm = pe.matmul(ps[4 + m], ctxT[s][:, k, m * P:(m + 1) * P], wkv[:, k, C:2 * C],
                                           start=(k == 0), stop=(k == KY - 1))
                        mm.then_inc(v_done, 1)

                def scores(b, s):
                    pe.wait_ge(qb_done, b + 1)
                    for c in range(KC):
                        pe.wait_ge(k_copied, b * KC + c + 1)
                        pe.matmul(ps[c][:, 0:M], q_blocks[s][:, c, :, :].rearrange("p h n -> p (h n)"), kT[s][:, c, :],
                                  start=True, stop=True).then_inc(s_done, 1)

                def apply(b, s, values_ahead):
                    pe.wait_ge(norm_done, b + 1)
                    for m in range(3):
                        if m > 0 and values_ahead:
                            pe.wait_ge(v_copied, (b + 1) * 2 + m)
                        rows = P if m < 2 else 1
                        bank = [6, 4, 5][m]
                        for c in range(KC):
                            mm = pe.transpose(ps[bank][0:rows, c * P:(c + 1) * P], prob[s][:, c, m * P:m * P + rows],
                                              ident[:, :])
                        mm.then_inc(t_done, 1)
                    pe.wait_ge(t_copied, (b + 1) * 3)
                    if not first(b):
                        pe.wait_ge(o_taken, b)
                    for c in range(KC):
                        cols = slice(c * P, (c + 1) * P)
                        for m in range(2):
                            pe.matmul(ps[7][:, cols], val[s][:, m, cols], probT[s][:, m, cols], start=(m == 0), stop=False)
                        mm = pe.matmul(ps[7][:, cols], v_tail[s][:, cols], probT_tail[s][:, cols], start=False, stop=True)
                    mm.then_inc(o_done, 1)

                keys_values(0, 0, 0)
                scores(0, 0)
                keys_values(1, 1, 0)
                apply(0, 0, True)
                scores(1, 1)
                with pe.Fori(0, B // 2 - 1) as i:
                    keys_values(i * 2 + 2, 0, i + 1)
                    apply(i * 2 + 1, 1, True)
                    scores(i * 2 + 2, 0)
                    keys_values(i * 2 + 3, 1, i + 1)
                    apply(i * 2 + 2, 0, True)
                    scores(i * 2 + 3, 1)
                apply(B - 1, 1, False)

            @block.scalar
            def _(act):
                def step(b, s, r):
                    for c in range(KC):
                        act.wait_ge(k_done, b * KC + c + 1)
                        nc.scalar.copy(kT[s][:, c, :], ps[c][:, 0:M]).then_inc(k_copied, 1)
                    if not (isinstance(b, int) and b < 2):
                        act.wait_ge(o_done, b - 1)
                    for m in range(2):
                        act.wait_ge(v_done, b * 2 + m + 1)
                        nc.scalar.copy(val[s][:, m, :], ps[4 + m]).then_inc(v_copied, 1)
                    for c in range(KC):
                        act.wait_ge(max_done, b * KC + c + 1)
                        nc.scalar.activation(prob[s][:, c, :], ps[c][:, 0:M], ACT.Exp, bias=neg_max[s][:, c:c + 1],
                                             accum_out=total[s][:, c:c + 1]).then_inc(exp_done, 1)

                batches(act, step)

            @block.vector
            def _(dve):
                def spread_queries(b, s):
                    if not (isinstance(b, int) and b < 2):
                        dve.wait_ge(s_done, (b - 1) * KC)
                    q = qT[:, :, bass.ds(b * N, N)]
                    nc.vector.tensor_tensor(q_blocks[s][:, :, :, :], q[:, :, None, :].to_broadcast([P, KC, HG, N]),
                                            block_mask[:, None, :, :].to_broadcast([P, KC, HG, N]),
                                            ALU.mult).then_inc(qb_done, 1)

                def softmax(b, s):
                    for c in range(KC):
                        dve.wait_ge(s_done, b * KC + c + 1)
                        nc.vector.tensor_reduce(neg_max[s][:, c:c + 1], ps[c][:, 0:M], AX.X, ALU.max,
                                                negate=True).then_inc(max_done, 1)
                    dve.wait_ge(exp_done, (b + 1) * KC)
                    nc.vector.reciprocal(total[s][:, :], total[s][:, :]).then_inc(recip_done, 1)
                    dve.wait_ge(recip_done, b + 1)
                    nc.vector.tensor_tensor(prob[s][:, :, :], prob[s][:, :, :],
                                            total[s][:, :, None].to_broadcast([P, KC, M]), ALU.mult).then_inc(norm_done, 1)

                def take(b, s):
                    for m in range(3):
                        dve.wait_ge(t_done, b * 3 + m + 1)
                        dst = probT[s][:, m, :] if m < 2 else probT_tail[s][:, :]
                        nc.vector.tensor_copy(dst, ps[[6, 4, 5][m]][0:P if m < 2 else 1, :]).then_inc(t_copied, 1)
                    dve.wait_ge(o_done, b + 1)
                    nc.vector.tensor_tensor(o_masked[:, :, :, :], ps[7].rearrange("p (c h n) -> p c h n", c=KC, h=HG),
                                            block_mask[:, None, :, :].to_broadcast([P, KC, HG, N]),
                                            ALU.mult).then_inc(masked_done, 1)
                    dve.wait_ge(masked_done, b + 1)
                    nc.vector.tensor_reduce(oT[:, :, bass.ds(b * N, N)], o_masked[:, :, :, :].rearrange("p c h n -> p c n h"),
                                            AX.X, ALU.add).then_inc(o_taken, 1)

                spread_queries(0, 0)
                spread_queries(1, 1)
                softmax(0, 0)
                take(0, 0)
                softmax(1, 1)
                with dve.Fori(0, B // 2 - 1) as i:
                    spread_queries(i * 2 + 2, 0)
                    take(i * 2 + 1, 1)
                    softmax(i * 2 + 2, 0)
                    spread_queries(i * 2 + 3, 1)
                    take(i * 2 + 2, 0)
                    softmax(i * 2 + 3, 1)
                take(B - 1, 1)


def project(nc, d, ps, ident, xnT, v_nat):
    with ExitStack() as ctx:
        sb = lambda name, shape: ctx.enter_context(nc.sbuf_tensor(name, shape, F32))
        sem = lambda name: ctx.enter_context(nc.semaphore(name))
        w = [sb(f"pw{n}", [P, KC, H * DK]) for n in "kqv"]
        bias = sb("p_bias", [P, 3, HC])
        w_gates = sb("w_gates", [P, KC, NG * H])
        g_bias, g_bias2 = sb("g_bias", [NG * H, 1]), sb("g_bias2", [NG * H, 1])
        head_cols = sb("head_cols", [P, HC, H])
        kqT = sb("kqT", [P, HC, 2, HALF])
        vT = sb("vT", [P, HC, HALF])
        q_sq = [sb(f"q_sq{s}", [P, HALF]) for s in range(2)]
        gates = sb("gates", [NG * H, TOK])
        qq = sb("qq", [H, TOK])
        gram = [sb(f"gram{s}", [P, HC, 2, 3, N]) for s in range(2)]
        w_in = [sem(f"pw_in{n}") for n in "kqvg"]
        zeroed, consts, bias_done = sem("g_zeroed"), sem("p_consts"), sem("g_bias_done")
        pj_done, pj_used, sq_done, qq_mm, qq_used = sem("pj_done"), sem("pj_used"), sem("sq_done"), sem("qq_mm"), sem("qq_used")
        pair_done, pair_dve, pair_act = sem("pair_done"), sem("pair_dve"), sem("pair_act")
        gram_out = [sem(f"gram_out{s}") for s in range(2)]
        gates_out = sem("gates_out")
        JOBS = 3 * HC + 1
        PAIRS = 7
        PJ_BANK = [0, 1, 7]

        with nc.Block() as block:
            @block.sync
            def _(sp):
                sp.dma_start(w[0][:, :, :], d["Wk"].rearrange("(k p) n -> p k n", p=P)).then_inc(w_in[0], 16)
                for n, name in enumerate(("bk", "bq", "bv")):
                    sp.dma_start(bias[:, n, :], d[name]).then_inc(w_in[0], 16)
                sp.dma_start(w[1][:, :, :], d["Wq"].rearrange("(k p) n -> p k n", p=P)).then_inc(w_in[1], 16)
                for g, name in enumerate(("b", "fd", "sd", "fg", "sg")):
                    sp.dma_start(w_gates[:, :, g * H:(g + 1) * H],
                                 d["W" + name].rearrange("(k p) h -> p k h", p=P)).then_inc(w_in[3], 16)
                    sp.dma_start(g_bias[g * H:(g + 1) * H, :], d["b" + name]).then_inc(w_in[3], 16)
                sp.wait_ge(zeroed, 1)
                sp.dma_start(g_bias2[H:2 * H, :], d["fast_decay_bias"]).then_inc(w_in[3], 16)
                sp.dma_start(g_bias2[2 * H:3 * H, :], d["slow_decay_bias"]).then_inc(w_in[3], 16)
                sp.dma_start(w[2][:, :, :], d["Wv"].rearrange("(k p) n -> p k n", p=P)).then_inc(w_in[2], 16)
                for t in range(NT):
                    sp.wait_ge(pair_dve, t * PAIRS + 6)
                    sp.wait_ge(pair_act, t * PAIRS + 6)
                    sp.dma_start(d["gram"][t * P:(t + 1) * P, :],
                                 gram[t % 2][:, :, :, :, :].rearrange("p c a e n -> p (c a e n)")).then_inc(gram_out[t % 2], 16)
                sp.wait_ge(pj_used, 2 * JOBS)
                sp.wait_ge(qq_used, 2)
                sp.dma_start(d["gates"][0:NG * H, :], gates[:, :]).then_inc(gates_out, 16)
                sp.dma_start(d["gates"][NG * H:(NG + 1) * H, :], qq[:, :]).then_inc(gates_out, 16)
                sp.wait_ge(gates_out, 32)
                for s in range(2):
                    sp.wait_ge(gram_out[s], 16 * NT // 2)

            @block.gpsimd
            def _(pool):
                nc.gpsimd.memset(g_bias2[:, :], 0.0).then_inc(zeroed, 1)
                nc.gpsimd.memset(head_cols[:, :, :], 0.0).then_inc(consts, 1)
                pool.wait_ge(consts, 1)
                for c in range(HC):
                    for a in range(2):
                        nc.gpsimd.memset(head_cols[a * DK:(a + 1) * DK, c, 2 * c + a:2 * c + a + 1], 1.0).then_inc(consts, 1)

            def tile_cols(t):
                return slice((t % TH) * P, (t % TH + 1) * P)

            @block.tensor
            def _(pe):
                for hf in range(2):
                    cols = slice(hf * HALF, (hf + 1) * HALF)
                    n = hf * JOBS
                    for part in (0, 1, 3, 2):
                        if hf == 0:
                            pe.wait_ge(w_in[part], [64, 16, 16, 16 * (2 * NG + 2)][part])
                        for c in range(HC if part < 3 else 1):
                            if n >= 3:
                                pe.wait_ge(pj_used, n - 2)
                            for k in range(KC):
                                if part < 3:
                                    mm = pe.matmul(ps[PJ_BANK[n % 3]], w[part][:, k, c * P:(c + 1) * P], xnT[:, k, cols],
                                                   start=(k == 0), stop=(k == KC - 1))
                                else:
                                    mm = pe.matmul(ps[PJ_BANK[n % 3]][0:NG * H, :], w_gates[:, k, :], xnT[:, k, cols],
                                                   start=(k == 0), stop=(k == KC - 1))
                            mm.then_inc(pj_done, 1)
                            n += 1
                    pe.wait_ge(consts, 1 + 2 * HC)
                    if hf:
                        pe.wait_ge(qq_used, hf)
                    for c in range(HC):
                        pe.wait_ge(sq_done, hf * HC + c + 1)
                        pe.matmul(ps[6][0:H, :], head_cols[:, c, :], q_sq[c % 2][:, :],
                                  start=(c == 0), stop=(c == HC - 1)).then_inc(qq_mm, 1)
                    pe.wait_ge(pj_used, (hf + 1) * JOBS)
                    for t in range(hf * TH, (hf + 1) * TH):
                        tc = tile_cols(t)
                        for j in range(PAIRS):
                            m = t * PAIRS + j
                            if m >= 2:
                                pe.wait_ge(pair_dve, m - 1)
                                pe.wait_ge(pair_act, m - 1)
                            bank = [ps[2 + 2 * (m % 2)], ps[3 + 2 * (m % 2)]]
                            if j < 4:
                                for i in range(2):
                                    for a in range(2):
                                        rows = slice(a * DK, (a + 1) * DK)
                                        mm = pe.matmul(bank[a][:, i * 2 * P:(i + 1) * 2 * P], kqT[rows, 2 * j + i, 0, tc],
                                                       kqT[rows, 2 * j + i, :, tc], start=True, stop=True)
                            elif j < 6:
                                for i in range(4):
                                    for a in range(2):
                                        rows, c = slice(a * DK, (a + 1) * DK), (j - 4) * 4 + i
                                        mm = pe.matmul(bank[a][:, i * P:(i + 1) * P], vT[rows, c, tc], vT[rows, c, tc],
                                                       start=True, stop=True)
                            else:
                                for c in range(HC):
                                    mm = pe.transpose(bank[c // 4][:, (c % 4) * P:(c % 4 + 1) * P], vT[:, c, tc], ident[:, :])
                            mm.then_inc(pair_done, 1)

            def take_pair(eng, copy, a, t, j):
                m = t * PAIRS + j
                eng.wait_ge(pair_done, m + 1)
                bank = ps[2 + 2 * (m % 2) + a]
                used = pair_dve if a == 0 else pair_act
                if j == 0 and t >= 2:
                    eng.wait_ge(gram_out[t % 2], 16 * (t // 2))
                if j == 6:
                    copy(v_nat[:, t, a * 512:(a + 1) * 512], bank).then_inc(used, 1)
                    return
                for b in range(BT):
                    rows = slice(b * N, (b + 1) * N)
                    if j < 4:
                        dst = gram[t % 2][rows, 2 * j:2 * j + 2, a, 0:2, :]
                        src = bank.rearrange("p (i e b n) -> p i e b n", i=2, e=2, b=BT)[rows, :, :, b, :]
                    else:
                        dst = gram[t % 2][rows, (j - 4) * 4:(j - 3) * 4, a, 2, :]
                        src = bank.rearrange("p (i b n) -> p i b n", i=4, b=BT)[rows, :, b, :]
                    ins = copy(dst, src)
                ins.then_inc(used, 1)

            @block.vector
            def _(dve):
                dve.wait_ge(w_in[3], 16 * (2 * NG + 2))
                nc.vector.tensor_tensor(g_bias[:, :], g_bias[:, :], g_bias2[:, :], ALU.add).then_inc(bias_done, 1)
                for hf in range(2):
                    for c in range(HC):
                        dve.wait_ge(pj_used, hf * JOBS + HC + c + 1)
                        if hf * HC + c >= 2:
                            dve.wait_ge(qq_mm, hf * HC + c - 1)
                        nc.vector.tensor_tensor(q_sq[c % 2][:, :], kqT[:, c, 1, :], kqT[:, c, 1, :], ALU.mult).then_inc(sq_done, 1)
                    dve.wait_ge(qq_mm, (hf + 1) * HC)
                    nc.vector.tensor_copy(qq[:, hf * HALF:(hf + 1) * HALF], ps[6][0:H, :]).then_inc(qq_used, 1)
                    for t in range(hf * TH, (hf + 1) * TH):
                        for j in range(PAIRS):
                            take_pair(dve, nc.vector.tensor_copy, 0, t, j)

            @block.scalar
            def _(act):
                for hf in range(2):
                    cols = slice(hf * HALF, (hf + 1) * HALF)
                    if hf:
                        act.wait_ge(pair_done, hf * TH * PAIRS)
                    n = hf * JOBS
                    for part in (0, 1, 3, 2):
                        for c in range(HC if part < 3 else 1):
                            act.wait_ge(pj_done, n + 1)
                            if part == 3:
                                act.wait_ge(bias_done, 1)
                                nc.scalar.activation(gates[:, cols], ps[PJ_BANK[n % 3]][0:NG * H, :], ACT.Sigmoid,
                                                     bias=g_bias[:, 0:1]).then_inc(pj_used, 1)
                            else:
                                dst = vT[:, c, :] if part == 2 else kqT[:, c, part, :]
                                nc.scalar.activation(dst, ps[PJ_BANK[n % 3]], ACT.Silu,
                                                     bias=bias[:, part, c:c + 1]).then_inc(pj_used, 1)
                            n += 1
                    for t in range(hf * TH, (hf + 1) * TH):
                        for j in range(PAIRS):
                            take_pair(act, nc.scalar.copy, 1, t, j)


def recurrence(nc, d, hf):
    with ExitStack() as ctx:
        sb = lambda name, shape: ctx.enter_context(nc.sbuf_tensor(f"{name}_{hf}", shape, F32))
        sem = lambda name: ctx.enter_context(nc.semaphore(f"{name}_{hf}"))
        G = sb("r_gram", [P, SG, N, 3, N])
        gt = sb("r_gates", [P, SG, NG + 1, N])
        kk = sb("r_kk", [P, SG, N, N, 2])
        coef = sb("r_coef", [P, SG, N, 2 * N])
        outw = sb("r_outw", [P, SG, 2 * N, N])
        prod = sb("r_prod", [P, 2 * SG, N, 2 * N])
        rkq, inv = sb("r_rkq", [P, SG, 2, N]), sb("r_inv", [P, SG, 2, N])
        neg_beta = sb("r_nbeta", [P, SG, N])
        cf = sb("r_cf", [P, SG, N, 9])
        kap, tmp = sb("r_kap", [P, SG, N]), sb("r_tmp", [P, SG, N])
        rf = sb("r_rf", [P, 1])
        mix = sb("r_mix", [P, 3, 9])
        wz = sb("r_wz", [P, SG, N, 3, 9])
        z = sb("r_z", [P, SG, 9])
        phi = sb("r_phi", [P, SG, 2, 2 * N])
        psi = [sb(f"r_psi{i}", [P, SG, 2, 2 * N]) for i in range(2)]
        y = sb("r_y", [P, SG, 2, 2 * N])
        pred = sb("r_pred", [P, 2 * SG, N])
        vp = sb("r_vp", [P, 2 * SG, N])
        dots = sb("r_dots", [P, SG, 3, N])
        zz, n2 = sb("r_zz", [P, SG, 3, 9]), sb("r_n2", [P, SG, 3])
        nm, root, c2 = sb("r_nm", [P, SG, 2]), sb("r_root", [P, SG, 2]), sb("r_c2", [P, SG, 3])
        cap = [sb(f"r_cap{i}", [P, SG, 2]) for i in range(2)]
        cd = sb("r_cd", [P, SG, 2])
        cg, outs, outsum = sb("r_cg", [P, SG, 2]), sb("r_outs", [P, SG, 2, 2 * N]), sb("r_outsum", [P, SG, 2 * N])
        loaded, own, pool_own, sq_ready, sq_done, nm_ready, root_ready = (
            sem("r_loaded"), sem("r_own"), sem("r_pool"), sem("r_sqr"), sem("r_sqd"), sem("r_nmr"), sem("r_rootr"))
        psi_ready, out_done, stored, zeroed, coef_ready = sem("r_psir"), sem("r_outd"), sem("r_stored"), sem("r_zeroed"), sem("r_coefr")
        LOADS = 2 * SG * BS + 1
        POOL_STEPS = 4

        def bc(ap, shape):
            return ap.to_broadcast([P] + shape)

        with nc.Block() as block:
            @block.sync
            def _(sp):
                sp.dma_start(rf[:, :], d["rf"].to_broadcast([P, 1])).then_inc(loaded, 16)
                for s in range(SG):
                    for i in range(BS):
                        b = (hf * SG + s) * BS + i
                        rows = slice(i * H, (i + 1) * H)
                        sp.dma_start(G[rows, s, :, :, :].rearrange("h i e n -> h i (e n)"),
                                     d["gram"][b * N:(b + 1) * N, :].rearrange("i (h e) -> h i e", h=H)).then_inc(loaded, 16)
                        sp.dma_start(gt[rows, s, :, :],
                                     d["gates"].rearrange("(g h) t -> h g t", h=H)[:, :, b * N:(b + 1) * N]).then_inc(loaded, 16)
                sp.wait_ge(coef_ready, 1)
                sp.wait_ge(out_done, N * POOL_STEPS)
                for s in range(SG):
                    seq = slice((hf * SG + s) * P, (hf * SG + s + 1) * P)
                    sp.dma_start(d["coef"][seq, :], coef[:, s, :, :].rearrange("p j m -> p (j m)")).then_inc(stored, 16)
                    sp.dma_start(d["outw"][seq, :], outw[:, s, :, :].rearrange("p m t -> p (m t)")).then_inc(stored, 16)
                sp.wait_ge(stored, 32 * SG)

            @block.gpsimd
            def _(pool):
                nc.gpsimd.memset(coef[:, :, :, :], 0.0).then_inc(zeroed, 1)
                nc.gpsimd.memset(outw[:, :, :, :], 0.0).then_inc(zeroed, 1)
                nc.gpsimd.memset(z[:, :, 0:8], 0.0).then_inc(zeroed, 1)
                nc.gpsimd.memset(z[:, :, 8:9], 1.0).then_inc(zeroed, 1)
                nc.gpsimd.memset(phi[:, :, :, :], 0.0).then_inc(zeroed, 1)
                pool.wait_ge(zeroed, 5)
                nc.gpsimd.memset(phi[:, :, 0, 0:2 * N:2], 1.0).then_inc(zeroed, 1)
                nc.gpsimd.memset(phi[:, :, 1, 1:2 * N:2], 1.0).then_inc(zeroed, 1)
                for t in range(N):
                    m = 2 * (t + 1)
                    pool.wait_ge(psi_ready, t + 1)
                    n = t * POOL_STEPS
                    nc.gpsimd.tensor_tensor(cg[:, :, :], cap[t % 2][:, :, :], gt[:, :, 3:5, t], ALU.mult).then_inc(out_done, 1)
                    pool.wait_ge(out_done, n + 1)
                    nc.gpsimd.tensor_tensor(outs[:, :, :, 0:m], psi[t % 2][:, :, :, 0:m], bc(cg[:, :, :, None], [SG, 2, m]),
                                            ALU.mult).then_inc(out_done, 1)
                    pool.wait_ge(out_done, n + 2)
                    nc.gpsimd.tensor_tensor(outsum[:, :, 0:m], outs[:, :, 0, 0:m], outs[:, :, 1, 0:m], ALU.add).then_inc(out_done, 1)
                    pool.wait_ge(out_done, n + 3)
                    nc.gpsimd.tensor_tensor(outw[:, :, 0:m, t].rearrange("p s (i k) -> p s i k", k=2),
                                            outsum[:, :, 0:m].rearrange("p s (i k) -> p s i k", k=2),
                                            bc(G[:, :, 0:t + 1, 1, t][:, :, :, None], [SG, t + 1, 2]), ALU.mult).then_inc(out_done, 1)

            @block.scalar
            def _(act):
                act.wait_ge(sq_ready, 1)
                nc.scalar.activation(inv[:, :, :, :], rkq[:, :, :, :], ACT.Sqrt).then_inc(sq_done, 1)
                for t in range(N):
                    act.wait_ge(nm_ready, t + 1)
                    nc.scalar.activation(root[:, :, :], nm[:, :, :], ACT.Sqrt, scale=1.0 / DK ** 2).then_inc(root_ready, 1)

            @block.vector
            def _(dve):
                ch = Chain(dve, own)
                link = ch.link
                tt, ts, red = nc.vector.tensor_tensor, nc.vector.tensor_scalar, nc.vector.tensor_reduce
                Gf = G[:, :, :, :, :].rearrange("p s i e n -> p s (i e n)")
                diag = lambda e: Gf[:, :, e * N:e * N + (N - 1) * (3 * N + 1) + 1:3 * N + 1]

                dve.wait_ge(loaded, 16 * LOADS)
                dve.wait_ge(zeroed, 7)
                ts(rkq[:, :, 0, :], diag(0), 1e-6, None, ALU.add)
                ts(rkq[:, :, 1, :], gt[:, :, NG, :], 1e-6, None, ALU.add).then_inc(sq_ready, 1)
                rf1 = rf[:, 0:1]
                ts(mix[:, 0, 2:3], rf1, 0.0, 1.0, ALU.mult, ALU.add)
                ts(mix[:, 2, 4:5], rf1, 0.0, 1.0, ALU.mult, ALU.add)
                ts(mix[:, 0, 3:4], rf1, 2.0, None, ALU.mult)
                ts(mix[:, 2, 3:4], rf1, 2.0, None, ALU.mult)
                ts(mix[:, 1, 2:3], rf1, 1.0, None, ALU.mult)
                ts(mix[:, 1, 4:5], rf1, 1.0, None, ALU.mult)
                tt(mix[:, 0, 4:5], rf1, rf1, ALU.mult)
                tt(mix[:, 2, 2:3], rf1, rf1, ALU.mult)
                link(ts(mix[:, 1, 3:4], rf1, rf1, 1.0, ALU.mult, ALU.add))
                nc.vector.tensor_copy(mix[:, :, 5:8], mix[:, :, 2:5])
                red(mix[:, :, 8:9], mix[:, :, 2:5], AX.X, ALU.add)
                nc.vector.scalar_tensor_tensor(mix[:, :, 0], mix[:, :, 2], 2.0, mix[:, :, 3], ALU.mult, ALU.add)
                link(nc.vector.scalar_tensor_tensor(mix[:, :, 1], mix[:, :, 4], 2.0, mix[:, :, 3], ALU.mult, ALU.add))
                dve.wait_ge(sq_done, 1)
                link(nc.vector.reciprocal(rkq[:, :, :, :], inv[:, :, :, :]))
                for s in range(SG):
                    kkq = G[:, s, :, 0:2, :]
                    link(tt(kkq, kkq, bc(rkq[:, s, None, :, :], [N, 2, N]), ALU.mult))
                    link(tt(kkq.rearrange("p i e n -> p i (e n)"), kkq.rearrange("p i e n -> p i (e n)"),
                            bc(rkq[:, s, 0, :, None], [N, 2 * N]), ALU.mult))
                    tt_last = nc.vector.tensor_copy(kk[:, s, :, :, :], bc(G[:, s, :, 0, :][:, :, :, None], [N, N, 2]))
                beta = gt[:, :, 0, :]
                link(tt(kap[:, :, :], beta, beta, ALU.mult))
                link(tt(kap[:, :, :], kap[:, :, :], diag(0), ALU.mult))
                ts(neg_beta[:, :, :], beta, -1.0, None, ALU.mult)
                tt(cf[:, :, :, 0], beta, kap[:, :, :], ALU.subtract)
                tt(cf[:, :, :, 1], beta, kap[:, :, :], ALU.subtract)
                for i in range(2, 5):
                    for s in range(SG):
                        nc.vector.scalar_tensor_tensor(cf[:, s, :, i], beta[:, s, :], -2.0, kap[:, s, :], ALU.mult, ALU.add)
                fd, sd = gt[:, :, 1, :], gt[:, :, 2, :]
                tt(cf[:, :, :, 5], fd, fd, ALU.mult)
                tt(cf[:, :, :, 6], fd, sd, ALU.mult)
                tt(cf[:, :, :, 7], sd, sd, ALU.mult)
                link(tt(cf[:, :, :, 8], kap[:, :, :], diag(2), ALU.mult))
                for s in range(SG):
                    ins = tt(wz[:, s, :, :, :], bc(cf[:, s, :, None, :], [N, 3, 9]), bc(mix[:, None, :, :], [N, 3, 9]), ALU.mult)
                link(ins)

                for t in range(N):
                    m = 2 * t
                    if t:
                        link(tt(y[:, :, :, 0:m], phi[:, :, :, 0:m],
                                bc(kk[:, :, t, 0:t, :].rearrange("p s i k -> p s (i k)")[:, :, None, :], [SG, 2, m]), ALU.mult))
                        for st in range(2):
                            ins = tt(prod[:, st::2, 0:t, 0:m], coef[:, :, 0:t, 0:m],
                                     bc(y[:, :, st, None, 0:m], [SG, t, m]), ALU.mult)
                        link(ins)
                        link(red(pred[:, :, 0:t], prod[:, :, 0:t, 0:m], AX.X, ALU.add))
                        for st in range(2):
                            ins = tt(prod[:, st::2, 0:t + 1, 0:t], G[:, :, 0:t + 1, 2, 0:t],
                                     bc(pred[:, st::2, None, 0:t], [SG, t + 1, t]), ALU.mult)
                        link(tt(coef[:, :, 0:t, m:m + 2].rearrange("p s j k -> p s k j"),
                                pred[:, :, 0:t].rearrange("p (s k) j -> p s k j", k=2),
                                bc(neg_beta[:, :, t][:, :, None, None], [SG, 2, t]), ALU.mult))
                        link(red(vp[:, :, 0:t + 1], prod[:, :, 0:t + 1, 0:t], AX.X, ALU.add))
                    ins = nc.vector.tensor_copy(coef[:, :, t, m:m + 2], bc(beta[:, :, t][:, :, None], [SG, 2]))
                    if t == N - 1:
                        ins.then_inc(coef_ready, 1)
                    if t:
                        nc.vector.tensor_copy(z[:, :, 0:2], vp[:, :, t].rearrange("p (s k) -> p s k", k=2))
                        vpv = vp[:, :, 0:t].rearrange("p (s k) j -> p s k j", k=2)
                        tt(dots[:, :, 0:2, 0:t], vpv, bc(pred[:, 0::2, None, 0:t], [SG, 2, t]), ALU.mult)
                        link(tt(dots[:, :, 2, 0:t], vp[:, 1::2, 0:t], pred[:, 1::2, 0:t], ALU.mult))
                        link(red(z[:, :, 2:5], dots[:, :, :, 0:t], AX.X, ALU.add))
                    link(tt(zz[:, :, :, :], wz[:, :, t, :, :], bc(z[:, :, None, :], [SG, 3, 9]), ALU.mult))
                    link(red(n2[:, :, :], zz[:, :, :, :], AX.X, ALU.add))
                    ts(nm[:, :, :], n2[:, :, 0:3:2], 0.0, None, ALU.max).then_inc(nm_ready, 1)
                    if t >= 2:
                        dve.wait_ge(out_done, (t - 1) * POOL_STEPS)
                    u = t % 2
                    w = m + 2
                    nc.vector.scalar_tensor_tensor(psi[u][:, :, 0, 0:w], phi[:, :, 1, 0:w], rf1, phi[:, :, 0, 0:w], ALU.mult, ALU.add)
                    nc.vector.scalar_tensor_tensor(psi[u][:, :, 1, 0:w], phi[:, :, 0, 0:w], rf1, phi[:, :, 1, 0:w], ALU.mult, ALU.add)
                    dve.wait_ge(root_ready, t + 1)
                    link(ts(root[:, :, :], root[:, :, :], 1.0, None, ALU.max))
                    nc.vector.reciprocal(cap[u][:, :, :], root[:, :, :]).then_inc(psi_ready, 1)
                    dve.wait_ge(psi_ready, t + 1)
                    if t < N - 1:
                        tt(c2[:, :, 0:2], cap[u][:, :, :], bc(cap[u][:, :, 0:1], [SG, 2]), ALU.mult)
                        tt(c2[:, :, 2:3], cap[u][:, :, 1:2], cap[u][:, :, 1:2], ALU.mult)
                        link(tt(cd[:, :, :], cap[u][:, :, :], gt[:, :, 1:3, t + 1], ALU.mult))
                        tt(z[:, :, 5:8], n2[:, :, :], c2[:, :, :], ALU.mult)
                        link(tt(phi[:, :, :, 0:w], psi[u][:, :, :, 0:w], bc(cd[:, :, :, None], [SG, 2, w]), ALU.mult))


def outputs(nc, d, ps, x_nat, xnT, v_nat):
    with ExitStack() as ctx:
        sb = lambda name, shape: ctx.enter_context(nc.sbuf_tensor(name, shape, F32))
        sem = lambda name: ctx.enter_context(nc.semaphore(name))
        wg, wo = sb("wg", [P, KC, H * DK]), sb("wo", [P, HC, C])
        bg, w_norm, bo, eps = sb("bg", [P, HC]), sb("w_norm", [P, 1]), sb("bo", [P, C]), sb("o_eps", [P, 1])
        same_head = sb("same_head", [P, P])
        gT = sb("gT", [P, HC, TOK])
        coef = [sb(f"o_coef{s}", [P, H, 2 * N]) for s in range(2)]
        outw = [sb(f"o_outw{s}", [P, BT, HC, N]) for s in range(2)]
        u = sb("o_u", [P, BT, 512])
        o_sq, o_g, o_rms = sb("o_sq", [P, HC, P]), sb("o_g", [P, HC, P]), sb("o_rms", [P, HC, P])
        w_in, t_in = sem("ow_in"), [sem(f"ot_in{s}") for s in range(2)]
        consts, g_done, g_used = sem("o_consts"), sem("g_done"), sem("g_used")
        u_done, u_copied, o_done, o_squared, o_gated = sem("u_done"), sem("u_copied"), sem("oo_done"), sem("o_squared"), sem("o_gated")
        ss_done, rms_done, inv_done, normed, y_done, y_used = (sem("ss_done"), sem("rms_done"), sem("oinv_done"), sem("normed"),
                                                               sem("y_done"), sem("y_used"))
        x_bias = sem("x_bias")
        with nc.Block() as block:
            @block.sync
            def _(sp):
                sp.dma_start(wg[:, :, :], d["Wg"].rearrange("(k p) n -> p k n", p=P)).then_inc(w_in, 16)
                sp.dma_start(bg[:, :], d["bg"]).then_inc(w_in, 16)
                sp.dma_start(wo[:, :, :], d["Wo"].rearrange("(c p) n -> p c n", p=P)).then_inc(w_in, 16)
                for a in range(2):
                    sp.dma_start(w_norm[a * DK:(a + 1) * DK, :], d["onorm_w"]).then_inc(w_in, 16)
                sp.dma_start(bo[:, :], d["bo"].to_broadcast([P, C])).then_inc(w_in, 16)
                for t in range(NT):
                    s = t % 2
                    if t >= 2:
                        sp.wait_ge(o_done, t - 1)
                    for i in range(BT):
                        b = t * BT + i
                        sp.dma_start(coef[s][i * N:(i + 1) * N, :, :],
                                     d["coef"][b * H:(b + 1) * H, :].rearrange("h (j m) -> j h m", j=N)).then_inc(t_in[s], 16)
                        for a in range(2):
                            sp.dma_start(outw[s][a * DK:(a + 1) * DK, i, :, :],
                                         d["outw"][b * H:(b + 1) * H, :].rearrange("(c a) (m t) -> a m c t", a=2, t=N)[a]
                                         ).then_inc(t_in[s], 16)

            @block.gpsimd
            def _(pool):
                nc.gpsimd.memset(same_head[:, :], 0.0).then_inc(consts, 1)
                nc.gpsimd.memset(eps[:, :], EPS).then_inc(consts, 1)
                pool.wait_ge(consts, 2)
                for a in range(2):
                    nc.gpsimd.memset(same_head[a * DK:(a + 1) * DK, a * DK:(a + 1) * DK], 1.0).then_inc(consts, 1)

            @block.tensor
            def _(pe):
                pe.wait_ge(w_in, 96)
                for n in range(2 * HC):
                    c, hf = n % HC, n // HC
                    if n >= 4:
                        pe.wait_ge(g_used, n - 3)
                    for k in range(KC):
                        mm = pe.matmul(ps[n % 4], wg[:, k, c * P:(c + 1) * P], xnT[:, k, hf * HALF:(hf + 1) * HALF],
                                       start=(k == 0), stop=(k == KC - 1))
                    mm.then_inc(g_done, 1)
                pe.wait_ge(g_used, 2 * HC)
                pe.wait_ge(consts, 4)
                for t in range(NT):
                    s = t % 2
                    pe.wait_ge(t_in[s], 16 * 3 * BT * (t // 2 + 1))
                    if t:
                        pe.wait_ge(y_used, t)
                    for h in range(H):
                        for i in range(BT):
                            rows = slice(i * N, (i + 1) * N)
                            a, c = h % 2, h // 2
                            mm = pe.matmul(ps[i][a * DK:(a + 1) * DK, c * DK:(c + 1) * DK], coef[s][rows, h, :],
                                           v_nat[rows, t, h * DK:(h + 1) * DK], start=True, stop=True)
                    mm.then_inc(u_done, 1)
                    pe.wait_ge(u_copied, BT * (t + 1))
                    if t:
                        pe.wait_ge(o_gated, 4 * t)
                        pe.wait_ge(o_squared, 4 * t)
                    for i in range(BT):
                        for c in range(HC):
                            for a in range(2):
                                rows = slice(a * DK, (a + 1) * DK)
                                col = (c % 4) * P + i * N
                                mm = pe.matmul(ps[4 + 2 * a + c // 4][rows, col:col + N], u[rows, i, c * DK:(c + 1) * DK],
                                               outw[s][rows, i, c, :], start=True, stop=True)
                    mm.then_inc(o_done, 1)
                    pe.wait_ge(o_squared, 4 * (t + 1))
                    for i in range(2):
                        pe.matmul(ps[i], same_head[:, :], o_sq[:, 4 * i:4 * i + 4, :].rearrange("p c n -> p (c n)"),
                                  start=True, stop=True).then_inc(ss_done, 1)
                    pe.wait_ge(normed, t + 1)
                    for c in range(HC):
                        mm = pe.matmul(ps[2], o_g[:, c, :], wo[:, c, :], start=(c == 0), stop=(c == HC - 1))
                    mm.then_inc(y_done, 1)

            @block.scalar
            def _(act):
                act.wait_ge(w_in, 96)
                for n in range(2 * HC):
                    c, hf = n % HC, n // HC
                    act.wait_ge(g_done, n + 1)
                    nc.scalar.activation(gT[:, c, hf * HALF:(hf + 1) * HALF], ps[n % 4], ACT.Silu, bias=bg[:, c:c + 1]).then_inc(g_used, 1)
                act.wait_ge(consts, 4)
                for t in range(NT):
                    act.wait_ge(u_done, t + 1)
                    for i in range(BT):
                        nc.scalar.copy(u[:, i, :], ps[i]).then_inc(u_copied, 1)
                    act.wait_ge(o_done, t + 1)
                    if t:
                        act.wait_ge(ss_done, 2 * t)
                    for a in range(2):
                        for i in range(2):
                            rows = slice(a * DK, (a + 1) * DK)
                            nc.scalar.activation(o_sq[rows, 4 * i:4 * i + 4, :].rearrange("p c n -> p (c n)"),
                                                 ps[4 + 2 * a + i][rows, :], ACT.Square).then_inc(o_squared, 1)
                    for i in range(2):
                        act.wait_ge(ss_done, 2 * t + i + 1)
                        if t and i == 0:
                            act.wait_ge(normed, t)
                        nc.scalar.activation(o_rms[:, 4 * i:4 * i + 4, :].rearrange("p c n -> p (c n)"), ps[i], ACT.Sqrt,
                                             scale=1.0 / DK, bias=eps[:, 0:1]).then_inc(rms_done, 1)

            @block.vector
            def _(dve):
                dve.wait_ge(w_in, 96)
                dve.wait_ge(g_used, 2 * HC)
                for t in range(NT):
                    nc.vector.tensor_tensor(x_nat[:, t, :], x_nat[:, t, :], bo[:, :], ALU.add).then_inc(x_bias, 1)
                    dve.wait_ge(o_done, t + 1)
                    if t:
                        dve.wait_ge(y_done, t)
                    for a in range(2):
                        for i in range(2):
                            rows = slice(a * DK, (a + 1) * DK)
                            dve.wait_ge(o_squared, 4 * t + 2 * a + i + 1)
                            nc.vector.tensor_tensor(o_g[rows, 4 * i:4 * i + 4, :],
                                                    ps[4 + 2 * a + i][rows, :].rearrange("p (c n) -> p c n", c=4),
                                                    gT[rows, 4 * i:4 * i + 4, t * P:(t + 1) * P], ALU.mult).then_inc(o_gated, 1)
                    dve.wait_ge(rms_done, 2 * (t + 1))
                    nc.vector.reciprocal(o_rms[:, :, :], o_rms[:, :, :]).then_inc(inv_done, 1)
                    dve.wait_ge(inv_done, t + 1)
                    dve.wait_ge(o_gated, 4 * (t + 1))
                    nc.vector.scalar_tensor_tensor(o_g[:, :, :], o_rms[:, :, :], w_norm[:, 0:1], o_g[:, :, :],
                                                   ALU.mult, ALU.mult).then_inc(normed, 1)
                    dve.wait_ge(y_done, t + 1)
                    dve.wait_ge(x_bias, t + 1)
                    nc.vector.tensor_tensor(x_nat[:, t, :], x_nat[:, t, :], ps[2], ALU.add).then_inc(y_used, 1)


def delta_rule(nc, d, ps, ident, x_nat, xnT):
    with nc.sbuf_tensor("v_nat", [P, NT, H * DK], F32) as v_nat:
        project(nc, d, ps, ident, xnT, v_nat)
        for hf in range(2):
            recurrence(nc, d, hf)
        outputs(nc, d, ps, x_nat, xnT, v_nat)
    layer_norm(nc, "n3_", x_nat, xnT, ident, ps)


SCRATCH = {"v_last": (B, C), "gram": (TOK, H * 3 * N), "gates": ((NG + 1) * H, TOK),
           "coef": (B * H, N * 2 * N), "outw": (B * H, 2 * N * N)}


def route(nc, d, ps, xnT, weight):
    with ExitStack() as ctx:
        sb = lambda name, shape: ctx.enter_context(nc.sbuf_tensor(name, shape, F32))
        sem = lambda name: ctx.enter_context(nc.semaphore(name))
        router = sb("router", [P, KC, E])
        order = sb("order", [P, E])
        s, best, at_best, first = sb("s", [P, NT, E]), sb("best", [P, NT]), sb("at_best", [P, NT, E]), sb("first", [P, NT])
        top, chosen, left, e = sb("top", [P, NT, E]), sb("chosen", [P, NT, E]), sb("left", [P, NT, E]), sb("expd", [P, NT, E])
        total = sb("r_total", [P, NT])
        w_in, consts, scored, own, shifted, exp_done = sem("rt_in"), sem("rt_consts"), sem("scored"), sem("rt_own"), sem("shifted"), sem("rt_exp")
        wide = lambda ap: ap[:, :, None].to_broadcast([P, NT, E])
        with nc.Block() as block:
            @block.sync
            def _(sp):
                sp.dma_start(router[:, :, :], d["router_w"].rearrange("(k p) e -> p k e", p=P)).then_inc(w_in, 16)

            @block.gpsimd
            def _(pool):
                for x in range(E):
                    nc.gpsimd.memset(order[:, x:x + 1], float(E - x)).then_inc(consts, 1)

            @block.tensor
            def _(pe):
                pe.wait_ge(w_in, 16)
                for t in range(NT):
                    for k in range(KC):
                        mm = pe.matmul(ps[0][:, t * E:(t + 1) * E], xnT[:, k, t * P:(t + 1) * P], router[:, k, :],
                                       start=(k == 0), stop=(k == KC - 1))
                mm.then_inc(scored, 1)

            @block.scalar
            def _(act):
                act.wait_ge(shifted, 1)
                nc.scalar.activation(e[:, :, :], e[:, :, :], ACT.Exp).then_inc(exp_done, 1)

            @block.vector
            def _(dve):
                link = Chain(dve, own).link
                tt, red = nc.vector.tensor_tensor, nc.vector.tensor_reduce
                dve.wait_ge(scored, 1)
                dve.wait_ge(consts, E)
                link(nc.vector.tensor_copy(s[:, :, :], ps[0][:, 0:NT * E].rearrange("p (t e) -> p t e", e=E)))
                link(nc.vector.tensor_copy(left[:, :, :], s[:, :, :]))
                for rank in range(2):
                    link(red(best[:, :], left[:, :, :], AX.X, ALU.max))
                    if rank == 0:
                        tt(e[:, :, :], s[:, :, :], wide(best), ALU.subtract).then_inc(shifted, 1)
                    link(tt(at_best[:, :, :], left[:, :, :], wide(best), ALU.is_equal))
                    link(tt(at_best[:, :, :], at_best[:, :, :], order[:, None, :].to_broadcast([P, NT, E]), ALU.mult))
                    link(red(first[:, :], at_best[:, :, :], AX.X, ALU.max))
                    link(tt(top[:, :, :], at_best[:, :, :], wide(first), ALU.is_equal))
                    if rank == 0:
                        link(nc.vector.tensor_copy(chosen[:, :, :], top[:, :, :]))
                        link(nc.vector.scalar_tensor_tensor(left[:, :, :], top[:, :, :], -3e38, left[:, :, :], ALU.mult, ALU.add))
                    else:
                        link(tt(chosen[:, :, :], chosen[:, :, :], top[:, :, :], ALU.add))
                dve.wait_ge(exp_done, 1)
                link(tt(e[:, :, :], e[:, :, :], chosen[:, :, :], ALU.mult))
                link(red(total[:, :], e[:, :, :], AX.X, ALU.add))
                link(nc.vector.reciprocal(total[:, :], total[:, :]))
                link(tt(weight[:, :, :], e[:, :, :], wide(total), ALU.mult))


def experts(nc, d, ps, ident, x_nat, xnT, out):
    with ExitStack() as ctx:
        sb = lambda name, shape, dt=F32: ctx.enter_context(nc.sbuf_tensor(name, shape, dt))
        sem = lambda name: ctx.enter_context(nc.semaphore(name))
        weight = sb("weight", [P, NT, E])
        route(nc, d, ps, xnT, weight)
        x_hi, x_lo = sb("x_hi", [P, KC, TOK], F32R), sb("x_lo", [P, KC, TOK], F32R)
        raw = [sb(f"w_raw{s}", [P, 3, 512]) for s in range(2)]
        w_hi = [sb(f"w_hi{s}", [P, 3, 512], F32R) for s in range(4)]
        w_lo = [sb(f"w_lo{s}", [P, 3, 512], F32R) for s in range(4)]
        silu = [sb(f"silu{s}", [P, HALF]) for s in range(2)]
        hid = [sb(f"hid{s}", [P, HALF]) for s in range(2)]
        h_hi = [sb(f"h_hi{s}", [P, HALF], F32R) for s in range(2)]
        h_lo = [sb(f"h_lo{s}", [P, HALF], F32R) for s in range(2)]
        raw_in = [sem(f"raw_in{s}") for s in range(2)]
        xh_done, xl_done, wh_done, wl_done = sem("xh_done"), sem("xl_done"), sem("wh_done"), sem("wl_done")
        gate_done, up_done, silu_done, hid_done, hh_done, hl_done, down_done, y_used, stored = (
            sem("gate_done"), sem("up_done"), sem("silu_done"), sem("hid_done"), sem("hh_done"), sem("hl_done"),
            sem("down_done"), sem("ey_used"), sem("stored"))
        STEPS = 2 * FC

        with nc.Block() as block:
            @block.sync
            def _(sp):
                for g in range(E * STEPS):
                    e, f, s = g // STEPS, g % FC, g % 2
                    if g >= 2:
                        sp.wait_ge(wl_done, g - 1)
                        sp.wait_ge(wh_done, g - 1)
                    cols = slice(f * P, (f + 1) * P)
                    for n, src in enumerate(("gate_proj", "up_proj")):
                        sp.dma_start(raw[s][:, n, :].rearrange("p (k f) -> p k f", k=KC),
                                     d[src][e][:, cols].rearrange("(k p) f -> p k f", p=P)).then_inc(raw_in[s], 16)
                    sp.dma_start(raw[s][:, 2, :], d["down_proj"][e][cols, :]).then_inc(raw_in[s], 16)
                sp.wait_ge(y_used, E * NT + TH)
                sp.dma_start(out.rearrange("b n c -> (b n) c").rearrange("(t p) c -> p t c", p=P), x_nat[:, :, :]).then_inc(stored, 16)
                sp.wait_ge(stored, 16)

            @block.tensor
            def _(pe):
                def gate_up(base, n):
                    hf, u = n // FC % 2, n % 2
                    pe.wait_ge(silu_done, base + n + 1)
                    pe.wait_ge(hid_done, base + n + 1)
                    pe.wait_ge(wh_done, base + n + 1)
                    pe.wait_ge(wl_done, base + n + 1)
                    for w, bank, done in ((0, ps[u], gate_done), (1, ps[2 + u], up_done)):
                        for k in range(KC):
                            hi, lo = w_hi[n % 4][:, w, k * P:(k + 1) * P], w_lo[n % 4][:, w, k * P:(k + 1) * P]
                            xh, xl = (x[:, k, hf * HALF:(hf + 1) * HALF] for x in (x_hi, x_lo))
                            pe.matmul(bank, hi, xh, start=(k == 0), stop=False)
                            pe.matmul(bank, hi, xl, start=False, stop=False)
                            mm = pe.matmul(bank, lo, xh, start=False, stop=(k == KC - 1))
                        mm.then_inc(done, 1)

                def down(base, pair, n):
                    half, f, u = n // FC, n % FC, n % 2
                    pe.wait_ge(hh_done, base + n + 1)
                    pe.wait_ge(hl_done, base + n + 1)
                    for j in range(TH):
                        if f == 0:
                            pe.wait_ge(y_used, pair * 2 * NT + half * TH + j + 1)
                        cols = slice(j * P, (j + 1) * P)
                        pe.matmul(ps[4 + j], h_hi[u][:, cols], w_hi[n % 4][:, 2, :], start=(f == 0), stop=False)
                        pe.matmul(ps[4 + j], h_hi[u][:, cols], w_lo[n % 4][:, 2, :], start=False, stop=False)
                        pe.matmul(ps[4 + j], h_lo[u][:, cols], w_hi[n % 4][:, 2, :], start=False,
                                  stop=(f == FC - 1)).then_inc(down_done, 1)

                pe.wait_ge(xh_done, KC)
                pe.wait_ge(xl_done, KC)
                with pe.Fori(0, E // 2) as pair:
                    base = pair * (2 * STEPS)
                    gate_up(base, 0)
                    for n in range(2 * STEPS):
                        if n + 1 < 2 * STEPS:
                            gate_up(base, n + 1)
                        down(base, pair, n)

            @block.scalar
            def _(act):
                def split_weights(g, u, r):
                    act.wait_ge(raw_in[u % 2], (r + 1) * 48)
                    if not (isinstance(g, int) and g < 4):
                        act.wait_ge(down_done, (g - 3) * TH)
                    nc.scalar.copy(w_hi[u][:, :, :], raw[u % 2][:, :, :]).then_inc(wh_done, 1)

                def hidden(g, v, ahead, r):
                    u = v % 2
                    act.wait_ge(gate_done, g + 1)
                    if not (isinstance(g, int) and g < 2):
                        act.wait_ge(hid_done, g + 1)
                    nc.scalar.activation(silu[u][:, :], ps[u], ACT.Silu).then_inc(silu_done, 1)
                    act.wait_ge(hid_done, g + 3)
                    nc.scalar.copy(h_hi[u][:, :], hid[u][:, :]).then_inc(hh_done, 1)
                    if ahead:
                        split_weights(g + 2, (v + 2) % 4, r + 1)

                act.sem_inc(silu_done, 2)
                for k in range(KC):
                    nc.scalar.copy(x_hi[:, k, :], xnT[:, k, :]).then_inc(xh_done, 1)
                split_weights(0, 0, 0)
                split_weights(1, 1, 0)
                for v in range(4):
                    hidden(v, v, True, v // 2)
                with act.Fori(1, E * STEPS // 4 - 1) as i:
                    for v in range(4):
                        hidden(i * 4 + v, v, True, i * 2 + v // 2)
                for v in range(4):
                    hidden(E * STEPS - 4 + v, v, v < 2, E * STEPS // 2 - 2 + v // 2)

            @block.vector
            def _(dve):
                def split_weights(g, u):
                    dve.wait_ge(wh_done, g + 1)
                    if not (isinstance(g, int) and g < 4):
                        dve.wait_ge(down_done, (g - 3) * TH)
                    nc.vector.tensor_tensor(w_lo[u][:, :, :], raw[u % 2][:, :, :], w_hi[u][:, :, :].bitcast(F32),
                                            ALU.subtract).then_inc(wl_done, 1)

                def hidden(base, n):
                    u = n % 2
                    dve.wait_ge(up_done, base + n + 1)
                    dve.wait_ge(silu_done, base + n + 3)
                    if not (isinstance(base, int) and base + n < 2):
                        dve.wait_ge(down_done, (base + n - 1) * TH)
                    nc.vector.tensor_tensor(hid[u][:, :], silu[u][:, :], ps[2 + u], ALU.mult).then_inc(hid_done, 1)
                    dve.wait_ge(hh_done, base + n + 1)
                    nc.vector.tensor_tensor(h_lo[u][:, :], hid[u][:, :], h_hi[u][:, :].bitcast(F32), ALU.subtract).then_inc(hl_done, 1)

                def add(base, pair, half):
                    for j in range(TH):
                        t = half % 2 * TH + j
                        dve.wait_ge(down_done, (base + (half + 1) * FC - 1) * TH + j + 1)
                        nc.vector.scalar_tensor_tensor(x_nat[:, t, :], ps[4 + j], weight[:, t, bass.ds(pair * 2 + half // 2, 1)],
                                                       x_nat[:, t, :], ALU.mult, ALU.add).then_inc(y_used, 1)

                def experts_pair(pair, last):
                    base = pair * (2 * STEPS)
                    for n in range(2 * STEPS):
                        hidden(base, n)
                        if n > 0 and n % FC == 0:
                            add(base, pair, n // FC - 1)
                        if not (last and n >= 2 * STEPS - 2):
                            split_weights(base + n + 2, (n + 2) % 4)
                    add(base, pair, 3)

                dve.sem_inc(hid_done, 2)
                dve.sem_inc(y_used, TH)
                for k in range(KC):
                    dve.wait_ge(xh_done, k + 1)
                    nc.vector.tensor_tensor(x_lo[:, k, :], xnT[:, k, :], x_hi[:, k, :].bitcast(F32), ALU.subtract).then_inc(xl_done, 1)
                split_weights(0, 0)
                split_weights(1, 1)
                experts_pair(0, False)
                with dve.Fori(1, E // 2 - 1) as pair:
                    experts_pair(pair, False)
                experts_pair(E // 2 - 1, True)


def perceiver_layer(nc, d, out):
    with ExitStack() as ctx:
        sb = lambda name, shape: ctx.enter_context(nc.sbuf_tensor(name, shape, F32))
        ps = [ctx.enter_context(nc.psum_tensor(f"bank{i}", [P, 512], F32))[:, :] for i in range(8)]
        ident = sb("ident", [P, P])
        x_nat = sb("x_nat", [P, NT, C])
        xnT = sb("xnT", [P, KC, TOK])
        mask_scale = sb("mask_scale", [P, NT])
        cross_attention(nc, d, ps, ident, x_nat, xnT, mask_scale)
        delta_rule(nc, d, ps, ident, x_nat, xnT)
        experts(nc, d, ps, ident, x_nat, xnT, out)




def kernel(**inputs):
    import numpy as np
    import concourse.bacc as bacc
    from concourse.bass_utils import run_bass_kernel_spmd as run

    a = {k: np.asarray(v) for k, v in inputs.items()}
    lay = np.ascontiguousarray
    arrays = {
        "x": lay(a["x"].reshape(TOK, C)),
        "mask": lay(a["mask_BxS_bk0"].reshape(NT, P).T),
        "ctxT": lay(a["ctx_768"].transpose(0, 2, 1)),
        "ctx_last": lay(a["ctx_768"][:, M - 1, :].T),
        "wqT": lay(a["L0_xattn_Wq"].T),
        "wkvT": lay(a["L0_xattn_Wkv"].T),
    }
    for name in ("Wq", "Wk", "Wv", "Wg", "Wo", "Wb", "Wfd", "Wsd", "Wfg", "Wsg"):
        arrays[name] = lay(a["L0_attn_" + name])
    for name in ("bq", "bk", "bv", "bg"):
        arrays[name] = lay(a["L0_attn_" + name].reshape(HC, P).T)
    for name in ("bb", "bfd", "bsd", "bfg", "bsg", "fast_decay_bias", "slow_decay_bias", "onorm_w"):
        arrays[name] = lay(a["L0_attn_" + name].reshape(-1, 1))
    arrays["bo"] = lay(a["L0_attn_bo"].reshape(1, C))
    arrays["rf"] = lay(a["L0_attn_resonance_flux"].reshape(1, 1))
    for name in ("router_w", "gate_proj", "up_proj", "down_proj"):
        arrays[name] = lay(a["L0_ffn_" + name])
    nc = bacc.Bacc("TRN2", target_bir_lowering=False, num_devices=1)
    d = {k: nc.dram_tensor("in_" + k, v.shape, mybir.dt.from_np(v.dtype), kind="ExternalInput").ap()
         for k, v in arrays.items()}
    for name, shape in SCRATCH.items():
        d[name] = nc.dram_tensor("scratch_" + name, shape, F32, kind="Internal").ap()
    out = nc.dram_tensor("out", (B, N, C), F32, kind="ExternalOutput").ap()
    perceiver_layer(nc, d, out)
    r = run(nc, [{"in_" + k: v for k, v in arrays.items()}], core_ids=[0])
    return r.results[0]["out"]
```
